# Optimizing a Trainium2 kernel written in Bass

```python
import numpy as np
import jax
import jax.numpy as jnp

def _softmax(x, axis=-1):
    return jax.nn.softmax(x, axis=axis)

def _gelu(x):
    return jax.nn.gelu(x, approximate=True)

def _silu(x):
    return jax.nn.silu(x)

def _sigmoid(x):
    return jax.nn.sigmoid(x)

def _layernorm(x, axis=-1, eps=1e-05):
    m = jnp.mean(x, axis=axis, keepdims=True)
    v = jnp.var(x, axis=axis, keepdims=True)
    return (x - m) / jnp.sqrt(v + eps)

def _scatter_add(tgt, idx, src, axis=0):
    return tgt.at[idx].add(src)

def _segment_sum(src, seg, n):
    return jax.ops.segment_sum(src, seg, n)
kernel_name = 'mk_gnn_resnorm_d4_gnn_r16_7552cf'

def setup_inputs(seed: int=0):
    np.random.seed(seed)
    _w = jnp.asarray

    def _rec_inputs():
        import jax
        import jax.numpy as jnp
        _gk = jax.random.key(seed)
        x = -0.0005121 + 1.001 * jax.random.normal(jax.random.fold_in(_gk, 1), (6250, 64), jnp.float32)
        src = jax.random.randint(jax.random.fold_in(_gk, 2), (200000,), 0, 6250, jnp.int32)
        dst = jnp.minimum((6250 * jax.random.uniform(jax.random.fold_in(_gk, 3), (200000,)) ** 2.0).astype(jnp.int32), 99999)
        _o = jnp.argsort(dst, stable=True)
        src = src[_o]
        dst = dst[_o]
        edge_attr_64 = -9.77346e-05 + 0.999888 * jax.random.normal(jax.random.fold_in(_gk, 12), (200000, 64), jnp.float32)
        edge_weight1 = jax.random.uniform(jax.random.fold_in(_gk, 14), (200000, 1), jnp.float32, 0.0, 0.999998)
        node_vec = jax.random.uniform(jax.random.fold_in(_gk, 15), (6250,), jnp.float32, 0.0, 0.999991)
        return (x, src, dst, edge_attr_64, edge_weight1, node_vec)
    x, src, dst, edge_attr_64, edge_weight1, node_vec = _rec_inputs()

    def _L0_gnn_setup():
        import jax, jax.numpy as jnp
        import numpy as np
        N_NODES = 3125
        N_EDGES = 50000
        NDIM_IN = 64
        EDIM = 64
        NDIM_OUT = 64
        key = jax.random.key(seed)
        ks = jax.random.split(key, 8)

        def xav(k, shape):
            fan_in, fan_out = (shape[0], shape[-1])
            std = np.sqrt(2.0) * np.sqrt(2.0 / (fan_in + fan_out))
            return jax.random.normal(k, shape, dtype=jnp.float32) * std
        return {'nfeats': jax.random.normal(ks[0], (N_NODES, NDIM_IN), dtype=jnp.float32), 'efeats': jax.random.normal(ks[1], (N_EDGES, EDIM), dtype=jnp.float32), 'W_ne': xav(ks[2], (NDIM_IN + EDIM, NDIM_OUT)), 'W_attn': xav(ks[3], (2 * NDIM_IN + EDIM, 1)), 'b_attn': jnp.zeros((1,), dtype=jnp.float32), 'W_out': xav(ks[4], (NDIM_IN + NDIM_OUT, NDIM_OUT)), 'src': jax.random.randint(ks[5], (N_EDGES,), 0, N_NODES, dtype=jnp.int64 if jax.config.jax_enable_x64 else jnp.int32), 'dst': jax.random.randint(ks[6], (N_EDGES,), 0, N_NODES, dtype=jnp.int64 if jax.config.jax_enable_x64 else jnp.int32)}
    _L0_gnn_all = _L0_gnn_setup()
    _L0_gnn_in = {k: v for k, v in _L0_gnn_all.items() if k in ('W_ne', 'W_attn', 'b_attn', 'W_out')}
    del _L0_gnn_all

    def _L1_gnn_setup():
        import jax, jax.numpy as jnp
        import numpy as np
        N_NODES = 3125
        N_EDGES = 50000
        IN_FEATS = 64
        N_HIDDEN = 16
        NUM_HEADS = 4

        def dot_gat_conv(feat, W, src, dst):
            n = feat.shape[0]
            ft = (feat @ W.T).reshape(n, NUM_HEADS, N_HIDDEN)
            ft_src = ft[src]
            e = (ft_src * ft[dst]).sum(-1) * (1.0 / np.sqrt(N_HIDDEN))
            m = jax.ops.segment_max(e, dst, num_segments=n)
            ex = jnp.exp(e - m[dst])
            z = jax.ops.segment_sum(ex, dst, num_segments=n)
            a = ex / z[dst]
            out = jax.ops.segment_sum(ft_src * a[:, :, None], dst, num_segments=n)
            return out.reshape(n, NUM_HEADS * N_HIDDEN)
        key = jax.random.key(seed)
        k1, k2, k3, k4, k5 = jax.random.split(key, 5)
        features = jax.random.normal(k1, (N_NODES, IN_FEATS), dtype=jnp.float32)
        edge_src = jax.random.randint(k2, (N_EDGES,), 0, N_NODES, dtype=jnp.int32)
        edge_dst = jax.random.randint(k3, (N_EDGES,), 0, N_NODES, dtype=jnp.int32)
        W1 = jax.random.normal(k4, (NUM_HEADS * N_HIDDEN, IN_FEATS), dtype=jnp.float32) * 0.1
        W2 = jax.random.normal(k5, (NUM_HEADS * N_HIDDEN, IN_FEATS), dtype=jnp.float32) * 0.1
        return {'features': features, 'edge_src': edge_src, 'edge_dst': edge_dst, 'W1': W1, 'W2': W2}
    _L1_gnn_all = _L1_gnn_setup()
    _L1_gnn_in = {k: v for k, v in _L1_gnn_all.items() if k in ('W1', 'W2')}
    del _L1_gnn_all

    def _L2_gnn_setup():
        import jax, jax.numpy as jnp
        import numpy as np
        N, E, D, K = (6250, 62500, 64, 2)

        def spline_conv(x, src, dst, u, W, lw, b):
            k = W.shape[0]
            v = u[:, 0] * (k - 1)
            i0 = jnp.clip(jnp.floor(v), 0, k - 1).astype(jnp.int32)
            frac = v - i0.astype(v.dtype)
            i1 = jnp.minimum(i0 + 1, k - 1)
            Z = jnp.einsum('ni,kio->nko', x, W)
            msg = (1.0 - frac)[:, None] * Z[src, i0] + frac[:, None] * Z[src, i1]
            agg = jax.ops.segment_sum(msg, dst, num_segments=x.shape[0])
            cnt = jax.ops.segment_sum(jnp.ones_like(dst, dtype=x.dtype), dst, num_segments=x.shape[0])
            out = agg / jnp.maximum(cnt, 1.0)[:, None]
            return out + x @ lw + b
        key = jax.random.key(seed)
        ks = jax.random.split(key, 10)
        x = jax.random.normal(ks[0], (N, D), dtype=jnp.float32)
        edge_index = jax.random.randint(ks[1], (2, E), 0, N, dtype=jnp.int64)
        edge_attr = jax.random.uniform(ks[2], (E, 1), dtype=jnp.float32)
        s = 1.0 / np.sqrt(D)
        W1 = jax.random.uniform(ks[3], (K, D, D), jnp.float32, -s, s)
        lw1 = jax.random.uniform(ks[4], (D, D), jnp.float32, -s, s)
        b1 = jnp.zeros((D,), jnp.float32)
        W2 = jax.random.uniform(ks[5], (K, D, D), jnp.float32, -s, s)
        lw2 = jax.random.uniform(ks[6], (D, D), jnp.float32, -s, s)
        b2 = jnp.zeros((D,), jnp.float32)
        return {'x': x, 'edge_index': edge_index, 'edge_attr': edge_attr, 'W1': W1, 'lw1': lw1, 'b1': b1, 'W2': W2, 'lw2': lw2, 'b2': b2}
    _L2_gnn_all = _L2_gnn_setup()
    _L2_gnn_in = {k: v for k, v in _L2_gnn_all.items() if k in ('W1', 'lw1', 'b1', 'W2', 'lw2', 'b2')}
    del _L2_gnn_all

    def _L3_gnn_setup():
        import jax, jax.numpy as jnp
        import numpy as np
        N_NODES = 6250
        N_EDGES = 100000
        DIM_IN = 64
        DIM_OUT = 64
        key = jax.random.key(seed)
        k1, k2, k3, k4 = jax.random.split(key, 4)
        x = jax.random.normal(k1, (N_NODES, DIM_IN), dtype=jnp.float32)
        edge_index = jax.random.randint(k2, (2, N_EDGES), 0, N_NODES, dtype=jnp.int32)
        edge_weight = jax.random.uniform(k3, (N_NODES,), dtype=jnp.float32)
        W = jax.random.normal(k4, (DIM_OUT, DIM_IN), dtype=jnp.float32) / np.sqrt(DIM_IN)
        return {'x': x, 'edge_index': edge_index, 'edge_weight': edge_weight, 'W': W}
    _L3_gnn_all = _L3_gnn_setup()
    _L3_gnn_in = {k: v for k, v in _L3_gnn_all.items() if k in ('W',)}
    del _L3_gnn_all
    return {'x': x, 'src': src, 'dst': dst, 'edge_attr_64': edge_attr_64, 'edge_weight1': edge_weight1, 'node_vec': node_vec, 'L0_gnn_W_ne': _L0_gnn_in['W_ne'], 'L0_gnn_W_attn': _L0_gnn_in['W_attn'], 'L0_gnn_b_attn': _L0_gnn_in['b_attn'], 'L0_gnn_W_out': _L0_gnn_in['W_out'], 'L1_gnn_W1': _L1_gnn_in['W1'], 'L1_gnn_W2': _L1_gnn_in['W2'], 'L2_gnn_W1': _L2_gnn_in['W1'], 'L2_gnn_lw1': _L2_gnn_in['lw1'], 'L2_gnn_b1': _L2_gnn_in['b1'], 'L2_gnn_W2': _L2_gnn_in['W2'], 'L2_gnn_lw2': _L2_gnn_in['lw2'], 'L2_gnn_b2': _L2_gnn_in['b2'], 'L3_gnn_W': _L3_gnn_in['W']}

def reference(x, src, dst, edge_attr_64, edge_weight1, node_vec, L0_gnn_W_ne, L0_gnn_W_attn, L0_gnn_b_attn, L0_gnn_W_out, L1_gnn_W1, L1_gnn_W2, L2_gnn_W1, L2_gnn_lw1, L2_gnn_b1, L2_gnn_W2, L2_gnn_lw2, L2_gnn_b2, L3_gnn_W):
    import jax
    import jax.numpy as jnp

    def _L0_gnn_ref(nfeats, efeats, W_ne, W_attn, b_attn, W_out, src, dst):
        import jax, jax.numpy as jnp
        import numpy as np
        N_NODES = 3125
        N_EDGES = 50000
        NDIM_IN = 64
        EDIM = 64
        NDIM_OUT = 64
        N = nfeats.shape[0]
        h_src = nfeats[src]
        h_dst = nfeats[dst]
        z_att = jnp.concatenate([h_src, h_dst, efeats], axis=-1)
        e = jax.nn.leaky_relu(z_att @ W_attn + b_attn, negative_slope=0.01)[:, 0]
        m = jnp.concatenate([h_src, efeats], axis=-1) @ W_ne
        emax = jax.ops.segment_max(e, dst, num_segments=N)
        ex = jnp.exp(e - emax[dst])
        denom = jax.ops.segment_sum(ex, dst, num_segments=N)
        alpha = ex / denom[dst]
        z = jax.ops.segment_sum(alpha[:, None] * m, dst, num_segments=N)
        out = jax.nn.relu(jnp.concatenate([nfeats, z], axis=-1) @ W_out)
        return out

    def _L1_gnn_ref(features, edge_src, edge_dst, W1, W2):
        import jax, jax.numpy as jnp
        import numpy as np
        N_NODES = 3125
        N_EDGES = 50000
        IN_FEATS = 64
        N_HIDDEN = 16
        NUM_HEADS = 4

        def dot_gat_conv(feat, W, src, dst):
            n = feat.shape[0]
            ft = (feat @ W.T).reshape(n, NUM_HEADS, N_HIDDEN)
            ft_src = ft[src]
            e = (ft_src * ft[dst]).sum(-1) * (1.0 / np.sqrt(N_HIDDEN))
            m = jax.ops.segment_max(e, dst, num_segments=n)
            ex = jnp.exp(e - m[dst])
            z = jax.ops.segment_sum(ex, dst, num_segments=n)
            a = ex / z[dst]
            out = jax.ops.segment_sum(ft_src * a[:, :, None], dst, num_segments=n)
            return out.reshape(n, NUM_HEADS * N_HIDDEN)
        h = dot_gat_conv(features, W1, edge_src, edge_dst)
        h = jax.nn.elu(h)
        h = dot_gat_conv(h, W2, edge_src, edge_dst)
        return h

    def _L2_gnn_ref(x, edge_index, edge_attr, W1, lw1, b1, W2, lw2, b2):
        import jax, jax.numpy as jnp
        import numpy as np
        N, E, D, K = (6250, 62500, 64, 2)

        def spline_conv(x, src, dst, u, W, lw, b):
            k = W.shape[0]
            v = u[:, 0] * (k - 1)
            i0 = jnp.clip(jnp.floor(v), 0, k - 1).astype(jnp.int32)
            frac = v - i0.astype(v.dtype)
            i1 = jnp.minimum(i0 + 1, k - 1)
            Z = jnp.einsum('ni,kio->nko', x, W)
            msg = (1.0 - frac)[:, None] * Z[src, i0] + frac[:, None] * Z[src, i1]
            agg = jax.ops.segment_sum(msg, dst, num_segments=x.shape[0])
            cnt = jax.ops.segment_sum(jnp.ones_like(dst, dtype=x.dtype), dst, num_segments=x.shape[0])
            out = agg / jnp.maximum(cnt, 1.0)[:, None]
            return out + x @ lw + b
        src, dst = (edge_index[0], edge_index[1])
        h = spline_conv(x, src, dst, edge_attr, W1, lw1, b1)
        h = jax.nn.relu(h)
        h = spline_conv(h, src, dst, edge_attr, W2, lw2, b2)
        h = jax.nn.relu(h)
        return h

    def _L3_gnn_ref(x, edge_index, edge_weight, W):
        import jax, jax.numpy as jnp
        import numpy as np
        N_NODES = 6250
        N_EDGES = 100000
        DIM_IN = 64
        DIM_OUT = 64
        n = x.shape[0]
        h = x @ W.T
        loop = jnp.arange(n, dtype=edge_index.dtype)
        dst = jnp.concatenate([edge_index[0], loop])
        src = jnp.concatenate([edge_index[1], loop])
        x_j = h[src] * edge_weight[src][:, None]
        h_prime = jax.ops.segment_sum(x_j, dst, num_segments=n)
        return h_prime
    edge_index = jnp.stack([src, dst])
    x = _layernorm(x + _L0_gnn_ref(x, edge_attr_64, L0_gnn_W_ne, L0_gnn_W_attn, L0_gnn_b_attn, L0_gnn_W_out, src, dst), axis=-1)
    x = _layernorm(x + _L1_gnn_ref(x, src, dst, L1_gnn_W1, L1_gnn_W2), axis=-1)
    x = _layernorm(x + _L2_gnn_ref(x, edge_index, edge_weight1, L2_gnn_W1, L2_gnn_lw1, L2_gnn_b1, L2_gnn_W2, L2_gnn_lw2, L2_gnn_b2), axis=-1)
    x = _layernorm(x + _L3_gnn_ref(x, edge_index, node_vec, L3_gnn_W), axis=-1)
    return x

_drawn_inputs = setup_inputs


def setup_inputs(seed=0):
    import zlib

    import numpy as np

    out = dict(_drawn_inputs(seed))
    spreads = {'L2_gnn_b1': (0.0, 0.1), 'L2_gnn_b2': (0.0, 0.1)}
    factors = {}
    for name, (base, spread) in spreads.items():
        noise = np.random.default_rng([zlib.crc32(name.encode()), seed]).standard_normal(out[name].shape)
        drawn = base * np.exp(spread * noise) if base else spread * noise
        out[name] = jnp.asarray(drawn.astype(out[name].dtype))
    for name, factor in factors.items():
        out[name] = (out[name] * factor).astype(out[name].dtype)
    return out
```

```python
import concourse.bass as bass
from concourse import mybir
from contextlib import ExitStack, contextmanager

N_NODES, D = 6250, 64
N_EDGES = 200000
P = 128
BLOCKS = -(-N_NODES // P)
TILES = -(-N_EDGES // P)
CH = 8
SUPER = 128
SUPERS = -(-(TILES + BLOCKS - 1) // SUPER)
STEPS = SUPERS * SUPER
CHUNKS = -(-(TILES + BLOCKS - 1) // CH)
SCH = SUPER // CH
LAST = CHUNKS - (SUPERS - 1) * SCH
SLOTS = SCH
TILES_PAD = STEPS
EF_TILES = STEPS - (BLOCKS - 1)
ROWS = 65
AC = 68
GB = 7
GROUPS = BLOCKS // GB
BANK = 512
BIG = 1e30
PAD_NODE = 1 << 20
LN_EPS = 1e-5
SB = BLOCKS + 1
TABLES = 2 * CH
assert LAST % 2 == 0 and GROUPS * GB == BLOCKS and GB * AC <= BANK


class Tally:

    def __init__(self, start=0):
        self.v, self.n = start, 0

    def next(self, k=1):
        self.v, self.n = self.v + k, self.n + k
        return self.v


@contextmanager
def loop(eng, count, pers):
    was = [(t, t.v, t.n, per) for t, per in pers]
    with eng.Fori(0, count) as i:
        for t, v, n, per in was:
            t.v = i * per + v
        yield i
        for k, (t, v, n, per) in enumerate(was):
            assert t.n - n == per, (k, t.n - n, per)
    for t, v, n, per in was:
        t.v, t.n = v + count * per, n + count * per


def gnn(nc, x_in, src_in, dst_in, u_in, eft_in, nv_in, w_ne, w_attn, b_attn, w_out,
        w1t, w2t, s_w1, s_lw1, s_b1, s_w2, s_lw2, s_b2, w3t, out):
    f32, i32, bf16 = mybir.dt.float32, mybir.dt.int32, mybir.dt.bfloat16
    ALU, ACT, AX = mybir.AluOpType, mybir.ActivationFunctionType, mybir.AxisListType
    X = AX.X
    V, A, T, G = nc.vector, nc.scalar, nc.tensor, nc.gpsimd
    ds = bass.ds
    ctx = ExitStack()
    with ctx:
        def sb(name, shape, dt=f32):
            return ctx.enter_context(nc.sbuf_tensor(name, shape, dt))

        def sem(name):
            return ctx.enter_context(nc.semaphore(name))

        def dram(name, shape, dt=f32):
            return nc.dram_tensor(name, shape, dt, kind="Internal").ap()

        tab0 = dram("tab0", [BLOCKS * P, 65])
        tab64 = [dram(f"tab64_{i}", [BLOCKS * P, D]) for i in range(2)]
        tab128 = [dram(f"tab128_{i}", [BLOCKS * P, 2 * D]) for i in range(2)]
        keyR_d = dram("keyR_d", [STEPS, P])
        keyC_d = dram("keyC_d", [P, STEPS])
        sums_d = [dram(f"sums_{t}", [P * SB, D]) for t in range(TABLES)]
        idx_d = dram("idx_d", [P, STEPS], i32)
        rel_d = dram("rel_d", [STEPS, P], bf16)
        NCOL = 6
        col_d = dram("col_d", [NCOL * SUPERS, P])
        C_TILE, C_POFS, C_SOFS, C_FIRST, C_LAST, C_RLAST = range(NCOL)

        xN = sb("xN", [P, BLOCKS * D])
        hN = sb("hN", [P, BLOCKS * D])
        linN = sb("linN", [P, BLOCKS * D])
        accS = sb("accS", [P, BLOCKS * AC])
        dstN = sb("dstN", [P, GROUPS * BANK])
        penF = sb("penF", [P, SUPERS * P + 1])
        penA = sb("penA", [P, SUPERS * P])
        penZ = sb("penZ", [P, SUPERS * P])
        relC = sb("relC", [P, STEPS])
        uC = sb("uC", [P, STEPS])
        invC = sb("invC", [P, STEPS])
        big = sb("big", [P, SUPER * ROWS])
        ring = sb("ring", [P, 8 * CH * ROWS])
        hot = sb("hot", [P, 2, CH * P])
        relrow = sb("relrow", [P, 2, CH * P], bf16)
        msg = sb("msg", [P, 2, CH, AC])
        msgF = msg[:, :, :, :].rearrange("p a b c -> p (a b c)")
        penS = msgF[:, 0:P + 1]
        penRS = msgF[0:4, 2 * P:4 * P + 1]
        hprev = msgF[0:4, 5 * P:6 * P]
        efs = sb("efs", [P, 2, CH, P])
        ef = efs[0:D, :, :, :]
        efR = efs[D:P, :, :, :]
        idxb = sb("idxb", [P, SLOTS, CH], i32)
        S = sb("S", [P, 4, P])
        R = sb("R", [P, 4, P])
        Fm = sb("Fm", [P, 4, P])
        Mx = sb("Mx", [P, 4, P])
        prod = Fm[:, :, :].rearrange("p a b -> p (a b)")
        rows33 = sb("rows33", [33, 2 * STEPS + 1])
        penR = rows33[0:4, :]
        offs = rows33[32:33, 0:2 * STEPS].bitcast(i32)
        seqK = sb("seqK", [4, 2, 2 * P])
        carry = sb("carry", [4, 1])
        small4 = sb("small4", [4, 12])
        prevrow = sb("prevrow", [4, 2, 16])
        prevofs = sb("prevofs", [1, 16], i32)
        AZ = sb("AZ", [P, 2, 4])
        fac = sb("fac", [P, 4])
        tmpP = ring[:, 0:GB * 2 * D]
        xT = ring[:, GB * 2 * D:GB * (2 * D + P)]
        nodev = sb("nodev", [P, 4, BLOCKS])
        den4 = sb("den4", [P, BLOCKS, 4])
        rcnt = sb("rcnt", [P, BLOCKS])
        nvS = sb("nvS", [P, BLOCKS])
        iotaF = sb("iotaF", [P, P])
        iotaP = sb("iotaP", [P, 1])
        ident = sb("ident", [P, P])
        prod2 = Mx[:, :, :].rearrange("p a b -> p (a b)")
        ones = Mx[:, 0, :]
        zeroW = sb("zeroW", [P, P], bf16)
        zeroM = sb("zeroM", [P, BANK], bf16)
        rhs0 = sb("rhs0", [D, 66])
        rhsE = sb("rhsE", [D, 65])
        rhsO = sb("rhsO", [2 * D, D])
        rhs1 = sb("rhs1", [D, 2, D])
        rhs2 = sb("rhs2", [D, 2, 3 * D])
        rhs3 = sb("rhs3", [D, D])
        biasS = sb("biasS", [P, 2, D])
        battn = sb("battn", [P, 1])
        permR = accS[:, STEPS:2 * STEPS]
        permC = hN[:, 0:STEPS]
        keyC = invC[:, :]
        keyrow = ring[:, 0:2 * CH * P].rearrange("p (a b) -> p a b", a=2)
        sums_out = ring[:, 2 * CH * P:2 * CH * (P + D)].rearrange("p (a b) -> p a b", a=2)
        h_edge = ring[:, 2 * CH * (P + D):2 * CH * (P + 2 * D)].rearrange("p (a b) -> p a b", a=2)
        same = big[:, 0:2 * CH * P].rearrange("p (a b) -> p a b", a=2)
        waste = big[:, 2 * CH * P:3 * CH * P]
        tri = Fm[:, 0, :]
        seen = Fm[:, 1, 0:CH]
        keep = Fm[:, 2, 0:CH]
        spare = Fm[:, 3, 0:1]
        sumsT = big[:, 0:2 * BLOCKS * D].rearrange("p (a b) -> p a b", a=2)
        n48 = BLOCKS - 1
        dstI = big[:, 0:SUPERS * P].bitcast(i32)
        keyF = big[:, SUPERS * P:2 * SUPERS * P]
        relF = big[:, 2 * SUPERS * P:3 * SUPERS * P]
        srcI = big[:, 3 * SUPERS * P:4 * SUPERS * P].bitcast(i32)
        srcF = hN[:, 0:STEPS]
        uR = linN[:, 0:STEPS]
        valR = accS[:, 0:STEPS]
        relB = dstN[:, 0:STEPS // 2].bitcast(bf16)
        firstR = dstN[0:4, STEPS // 2:STEPS // 2 + STEPS]
        lastR = accS[0:4, STEPS:2 * STEPS]
        idxF = ring[:, 0:STEPS]
        idxI = ring[:, STEPS:2 * STEPS].bitcast(i32)
        cmp = hot[:, 0, 0:n48 * SUPERS]
        assert 2 * STEPS <= 8 * CH * ROWS and n48 * SUPERS <= CH * P
        su = hot[:, 1, 0:6 * n48].rearrange("p (a b) -> p a b", b=n48)
        S_B128, S_CF, S_CL, S_RANK, S_DEAD, S_BM1 = range(6)
        sk = hot[:, 1, 512:512 + 10 * SUPERS].rearrange("p (a b) -> p a b", b=SUPERS)
        K_K, K_B, K_DEAD, K_BASE = 0, 1, 2, 3
        K_COL = 4
        tkI = hot[:, 1, 960:960 + SUPERS].bitcast(i32)
        firstlast = hot[:, 1, 768:768 + 2 * SUPERS].rearrange("p (a b) -> p a b", b=SUPERS)
        colT = hot[0:NCOL * SUPERS, 1, 800:800 + P]

        acc = ctx.enter_context(nc.psum_tensor("acc", [P, GROUPS, BANK], f32))
        accF = acc[:, :, :].rearrange("p a b -> p (a b)")
        sm = ctx.enter_context(nc.psum_tensor("sm", [P, BANK], f32))

        i_iota = sem("i_iota")
        i_dst = sem("i_dst")
        i_w = sem("i_w")
        i_tk = sem("i_tk")
        i_cntq = sem("i_cntq")
        i_cnt = sem("i_cnt")
        i_gd = sem("i_gd")
        i_gs = sem("i_gs")
        i_gu = sem("i_gu")
        i_row = sem("i_row")
        i_tr = sem("i_tr")
        i_trc = sem("i_trc")
        i_sc = sem("i_sc")
        i_ld = sem("i_ld")
        i_ready = sem("i_ready")
        i_idx = sem("i_idx")
        dve = sem("dve")
        act = sem("act")
        p_tmp = sem("p_tmp")
        p_tp = sem("p_tp")
        p_xT = sem("p_xT")
        p_o = sem("p_o")
        p_ev = sem("p_ev")
        n_src = sem("n_src")
        n_tab = sem("n_tab")
        n_exp = sem("n_exp")
        n_expd = sem("n_expd")
        g_idx = [sem(f"g_idx{j}") for j in range(SLOTS)]
        g_row = [sem(f"g_row{j}") for j in range(SLOTS)]
        r_dve = sem("r_dve")
        r_act = sem("r_act")
        l_rel = [sem(f"l_rel{j}") for j in range(2)]
        l_ef = [sem(f"l_ef{j}") for j in range(2)]
        ef_rdy = sem("ef_rdy")
        hot_rdy = sem("hot_rdy")
        d_rdy = sem("d_rdy")
        d_free = sem("d_free")
        s_rdy = sem("s_rdy")
        tr_rdy = sem("tr_rdy")
        tr_cp = sem("tr_cp")
        m_rows = sem("m_rows")
        m_rowsT = sem("m_rowsT")
        m_seq = sem("m_seq")
        m_seqT = sem("m_seqT")
        e_arg = sem("e_arg")
        e_rdy = sem("e_rdy")
        f_arg = sem("f_arg")
        f_exp = sem("f_exp")
        f_rhs = sem("f_rhs")
        f_all = sem("f_all")
        msg_rdy = sem("msg_rdy")
        b_free = sem("b_free")
        acc_rdy = sem("acc_rdy")
        acc_free = sem("acc_free")
        z_tab = sem("z_tab")
        w_tab = [sem(f"w_tab{j}") for j in range(2)]
        i_perm = sem("i_perm")
        k_room = sem("k_room")
        k_col = sem("k_col")
        k_free = sem("k_free")
        l_key = [sem(f"l_key{j}") for j in range(2)]
        same_rdy = sem("same_rdy")
        h_rdy = sem("h_rdy")
        t_rdy = sem("t_rdy")
        out_rdy = sem("out_rdy")
        idx_rdy = sem("idx_rdy")
        t_ld = [sem(f"t_ld{j}") for j in range(2)]
        t_use = sem("t_use")
        o_rdy = sem("o_rdy")
        o_done = sem("o_done")

        W_LOADS = 22

        LINKS = {1: 19, 4: 26}
        PASSES = [("ef", 1), ("dot", 4), ("dot", 4), ("spline", 0), ("spline", 0)]
        TABS = [tab0, tab64[0], tab64[1], tab128[0], tab128[1]]
        WIDTH = {"ef": 65, "dot": D, "spline": 2 * D}
        USE = {"ef": SLOTS, "dot": SLOTS, "spline": 4}
        hotB = hot[:, :, 0:CH * P // 2].bitcast(bf16)
        dstB = dstN[:, :].bitcast(bf16)

        def slot(kind, j, steps=slice(0, CH)):
            w = WIDTH[kind]
            home, j = (ring, j) if j < 8 else (linN, j - 8) if j < 14 else (hN, j - 14)
            v = home[:, j * CH * w:(j + 1) * CH * w].rearrange("p (s w) -> p s w", w=w)
            return v[:, steps, :]

        def load_values(engine, at, top, count=CH):
            out = []
            for q in range(0, count, 4):
                _, v = nc.values_load_multi_w_load_instructions(
                    offs[0:1, ds(at + q, min(4, count - q))], engines=[engine], min_val=0, max_val=top,
                    skip_runtime_bounds_check_because="worked out on the chip within these bounds")
                out += list(v)
            return out

        def hold(eng):
            eng.nop(nofuse=True)

        block = ctx.enter_context(nc.Block())

        @block.sync
        def _(sp):
            dst_v = dst_in.rearrange("(c p) e -> p c e", p=P)
            sp.dma_start(dstI.rearrange("p (c e) -> p c e", e=P), dst_v).then_inc(i_dst, 16)
            full = (N_NODES // P) * P
            rest = N_NODES - full
            xv = xN[:, :].rearrange("p (b d) -> p b d", d=D)
            sp.wait_ge(i_row, 1)
            loads = [
                (xv[:, 0:BLOCKS - 1, :], x_in[0:full, :].rearrange("(b p) d -> p b d", p=P)),
                (xv[0:rest, BLOCKS - 1, :], x_in[full:N_NODES, :]),
                (nvS[:, 0:BLOCKS - 1], nv_in[0:full].rearrange("(b p) -> p b", p=P)),
                (nvS[0:rest, BLOCKS - 1:BLOCKS], nv_in[full:N_NODES].rearrange("(p o) -> p o", o=1)),
                (rhs0[:, 0:D], w_ne[0:D, :]), (rhs0[:, D:D + 1], w_attn[0:D, :]),
                (rhs0[:, D + 1:D + 2], w_attn[D:2 * D, :]),
                (rhsE[:, 0:D], w_ne[D:2 * D, :]), (rhsE[:, D:D + 1], w_attn[2 * D:3 * D, :]),
                (rhsO[:, :], w_out),
                (rhs1[:, 0, :], w1t), (rhs1[:, 1, :], w2t),
                (rhs2[:, 0, 0:D], s_w1[0]), (rhs2[:, 0, D:2 * D], s_w1[1]), (rhs2[:, 0, 2 * D:], s_lw1),
                (rhs2[:, 1, 0:D], s_w2[0]), (rhs2[:, 1, D:2 * D], s_w2[1]), (rhs2[:, 1, 2 * D:], s_lw2),
                (rhs3[:, :], w3t),
                (biasS[:, 0, :], s_b1.partition_broadcast(P)), (biasS[:, 1, :], s_b2.partition_broadcast(P)),
                (battn[:, :], b_attn.partition_broadcast(P)),
            ]
            with nc.allow_non_contiguous_dma(reason="node weights, one float per partition"):
                for o, i in loads:
                    sp.dma_start(o, i).then_inc(i_w, 16)
            assert len(loads) == W_LOADS
            sp.wait_ge(i_row, 2)
            sp.dma_start(rel_d.rearrange("(c p) e -> p c e", p=P),
                         relB.rearrange("p (c e) -> p c e", e=P)).then_inc(i_sc, 16)
            sp.wait_ge(i_perm, 1)
            sp.dma_start(keyR_d.rearrange("(c p) e -> p c e", p=P),
                         permR.rearrange("p (c e) -> p c e", e=P)).then_inc(i_sc, 16)
            sp.wait_ge(i_idx, 1)
            sp.dma_start(idx_d, idxI).then_inc(i_sc, 16)
            sp.wait_ge(i_perm, 2)
            sp.dma_start(keyC_d, permC).then_inc(i_sc, 16)
            sp.wait_ge(i_trc, 3 * 4 + 4 + 1)
            sp.dma_start(col_d, colT).then_inc(i_sc, 16)
            sp.wait_ge(i_sc, 80)

            def col(c):
                return col_d[c * SUPERS:(c + 1) * SUPERS, :].rearrange("c p -> (c p)")

            def prev(c):
                return col_d[c * SUPERS:(c + 1) * SUPERS - 1, P - 1]

            sp.dma_start(firstR, col(C_FIRST).partition_broadcast(4)).then_inc(i_ld, 16)
            sp.dma_start(lastR, col(C_LAST).partition_broadcast(4)).then_inc(i_ld, 16)
            sp.dma_start(rows33[32:33, 0:STEPS], col(C_TILE).partition_broadcast(1)).then_inc(i_ld, 16)
            sp.dma_start(rows33[32:33, STEPS:2 * STEPS], col(C_POFS).partition_broadcast(1)).then_inc(i_ld, 16)
            with nc.allow_non_contiguous_dma(reason="one float of every super-step"):
                sp.dma_start(prevrow[:, 0, 1:SUPERS], prev(C_RLAST).partition_broadcast(4)).then_inc(i_ld, 16)
                sp.dma_start(prevrow[:, 1, 1:SUPERS], prev(C_SOFS).partition_broadcast(4)).then_inc(i_ld, 16)
            sp.wait_ge(i_ready, 1)
            for t in range(TABLES):
                tv = sums_d[t].rearrange("(p b) d -> p (b d)", p=P)
                sp.dma_start(tv[:, 0:BLOCKS * D], linN[:, :]).then_inc(z_tab, 16)
                sp.dma_start(tv[:, BLOCKS * D:SB * D], linN[:, 0:D]).then_inc(z_tab, 16)

            n_ev = Tally(1)
            tab = Tally()
            rel = [Tally() for _ in range(2)]
            free = {"r_dve": Tally(SLOTS), "r_act": Tally(SLOTS)}
            dots = Tally()
            for (kind, heads), table in zip(PASSES, TABS):
                w = WIDTH[kind]
                tv = table.rearrange("(b p) w -> p b w", p=P)
                with loop(sp, GROUPS, [(n_ev, 1), (tab, 16)]) as g:
                    sp.wait_ge(p_ev, n_ev.next())
                    hold(sp)
                    sp.dma_start(tv[:, ds(g * GB, GB), :],
                                 big[:, ds(g * (GB * w), GB * w)].rearrange("p (b w) -> p b w", w=w)
                                 ).then_inc(n_tab, 16)
                    tab.next(16)
                sp.wait_ge(n_tab, tab.v)
                if kind == "ef":
                    n_ev.next(GROUPS)
                relse = {"ef": [("r_dve", r_dve)], "dot": [("r_dve", r_dve), ("r_act", r_act)],
                         "spline": [("r_dve", r_dve)]}[kind]
                use = USE[kind]
                lag = use - 2 if heads else 0
                base = {name: free[name].v for name, _ in relse}

                def load_idx(n, j):
                    for name, s in relse:
                        sp.wait_ge(s, n + (base[name] + 1 - use))
                        hold(sp)
                    sp.dma_start(idxb[:, j, :], idx_d[:, ds(n * CH, CH)]).then_inc(g_idx[j], 16)

                def load_edges(m, j):
                    if kind == "dot":
                        sp.wait_ge(d_rdy, m + (dots.v - 1))
                    else:
                        sp.wait_ge(r_dve, m + (base["r_dve"] - 1))
                    hold(sp)
                    sp.dma_start(relrow[:, j % 2, :],
                                 rel_d[ds(m * CH, CH), :].rearrange("c p -> (c p)").partition_broadcast(P)
                                 ).then_inc(l_rel[j % 2], 16)

                def load_tiles(m, j):
                    t = sp.value_load(offs[0:1, ds(m * CH, 1)], min_val=0, max_val=EF_TILES - CH)
                    sp.wait_ge(ef_rdy, m + 1)
                    hold(sp)
                    sp.dma_start(efR[:, j % 2, :, :], eft_in[ds(t, CH), :, :].rearrange("o f e -> f o e")
                                 ).then_inc(l_ef[j % 2], 16)

                if heads:
                    for n in range(lag):
                        if kind == "ef" and n == 8:
                            sp.wait_ge(z_tab, 16 * 2 * TABLES)
                        load_idx(n, n)
                    if kind == "ef":
                        load_tiles(0, 0)
                    rounds = (CHUNKS - lag) // use
                    with sp.Fori(0, rounds) as i:
                        for j in range(use):
                            load_edges(i * use + j, j)
                            if kind == "ef":
                                load_tiles(i * use + j + 1, j + 1)
                            load_idx(i * use + j + lag, (j + lag) % use)
                    for m in range(rounds * use, CHUNKS):
                        j = m % use
                        load_edges(m, j)
                        if kind == "ef" and m + 1 < CHUNKS:
                            load_tiles(m + 1, j + 1)
                        if m + lag < CHUNKS:
                            load_idx(m + lag, (j + lag) % use)
                else:
                    with sp.Fori(0, CHUNKS // use) as i:
                        for j in range(use):
                            load_idx(i * use + j, j)
                    for m in range(CHUNKS // use * use, CHUNKS):
                        load_idx(m, m % use)
                for name, _ in relse:
                    free[name].next(CHUNKS)
                dots.next({"ef": 2, "dot": 1, "spline": 0}[kind] * CHUNKS)

            sp.wait_ge(k_room, 1)
            sp.dma_start(keyC, keyC_d).then_inc(k_col, 16)
            kf = Tally()
            with loop(sp, CHUNKS // 2, [(kf, 2)]) as i:
                for j in range(2):
                    sp.wait_ge(k_free, kf.next())
                    hold(sp)
                    m = i * 2 + j
                    sp.dma_start(relrow[:, j, :], rel_d[ds(m * CH, CH), :].rearrange("c p -> (c p)")
                                 .partition_broadcast(P)).then_inc(l_rel[j], 16)
                    sp.dma_start(keyrow[:, j, :], keyR_d[ds(m * CH, CH), :].rearrange("c p -> (c p)")
                                 .partition_broadcast(P)).then_inc(l_key[j], 16)
            for w in w_tab:
                sp.wait_ge(w, 16 * CH * CHUNKS // 2)
            for t in range(TABLES):
                sp.wait_ge(t_use, t + 1)
                sp.dma_start(sumsT[:, t % 2, :],
                             sums_d[t].rearrange("(p b) d -> p (b d)", p=P)[:, 0:BLOCKS * D]
                             ).then_inc(t_ld[t % 2], 16)

            full_o = out[0:full, :].rearrange("(b p) d -> p b d", p=P)
            sp.wait_ge(o_rdy, 1)
            sp.dma_start(full_o, xv[:, 0:BLOCKS - 1, :]).then_inc(o_done, 16)
            sp.dma_start(out[full:N_NODES, :], xv[0:rest, BLOCKS - 1, :]).then_inc(o_done, 16)
            sp.wait_ge(o_done, 32)

        @block.gpsimd
        def _(pool):
            G.iota(iotaF[:, :], [[1, P]], base=0, channel_multiplier=0,
                   allow_small_or_imprecise_dtypes=True).then_inc(i_iota, 1)
            G.iota(iotaP[:, :], [[0, 1]], base=0, channel_multiplier=1,
                   allow_small_or_imprecise_dtypes=True).then_inc(i_iota, 1)
            G.iota(sk[:, K_K, :], [[P, SUPERS]], base=0, channel_multiplier=1,
                   allow_small_or_imprecise_dtypes=True).then_inc(i_iota, 1)
            G.iota(su[:, S_B128, :], [[P, n48]], base=P, channel_multiplier=0,
                   allow_small_or_imprecise_dtypes=True).then_inc(i_iota, 1)
            pool.wait_ge(i_tk, 1)
            srcv = srcI.rearrange("p (c e) -> p c e", e=P)
            dstv = dstI.rearrange("p (c e) -> p c e", e=P)
            uv = uR.rearrange("p (c e) -> p c e", e=P)
            for o, i, s in ((dstv, dst_in, i_gd), (srcv, src_in, i_gs), (uv, u_in, i_gu)):
                for c in range(SUPERS):
                    pool.indirect_dma_start(o[:, c, :], None, i,
                                            bass.IndirectOffsetOnAxis(ap=tkI[:, c:c + 1], axis=0)
                                            ).then_inc(s, 16)
            got = [Tally() for _ in range(SLOTS)]
            for (kind, heads), table in zip(PASSES, TABS):
                use = USE[kind]

                def gather(slots):
                    for j in slots:
                        pool.wait_ge(g_idx[j], got[j].next(16))
                        hold(pool)
                        for r in range(CH):
                            pool.indirect_dma_start(slot(kind, j)[:, r, :], None, table,
                                                    bass.IndirectOffsetOnAxis(ap=idxb[:, j, r:r + 1], axis=0)
                                                    ).then_inc(g_row[j], 16)

                with loop(pool, CHUNKS // use, [(got[j], 16) for j in range(use)]):
                    gather(range(use))
                gather(range(CHUNKS % use))

            ready = Tally()
            with loop(pool, CHUNKS // 2, [(ready, 2)]) as i:
                for j in range(2):
                    ready.next()
                    pool.wait_ge(idx_rdy, ready.v)
                    hold(pool)
                    pool.wait_ge(out_rdy, ready.v)
                    hold(pool)
                    for r in range(CH):
                        pool.indirect_dma_start(sums_d[j * CH + r],
                                                bass.IndirectOffsetOnAxis(ap=idxb[:, j, r:r + 1], axis=0),
                                                sums_out[:, j, r * D:(r + 1) * D], None,
                                                compute_op=ALU.add).then_inc(w_tab[j], 16)

        @block.scalar
        def _(a):
            n_act, n_tr, n_srcT, n_tp = Tally(), Tally(), Tally(), Tally()
            t_tr, t_e, t_f, t_n, t_af = (Tally() for _ in range(5))
            t_rd = Tally(SLOTS - 2)
            efT = [Tally() for _ in range(2)]
            efRF = efR.rearrange("f a s e -> f a (s e)")
            rows = [Tally() for _ in range(SLOTS)]

            def quad(view, n):
                a.wait_ge(i_tr, n_tr.next())
                b = (n_tr.n - 1) % 4
                A.copy(view, acc[:, b, 0:view.shape[1]]).then_inc(i_trc, 1)

            for dest in (relC, invC, idxF, uC):
                for c in range(0, SUPERS, 4):
                    m = min(4, SUPERS - c)
                    quad(dest[:, c * P:(c + m) * P], m)
            a.wait_ge(i_tr, n_tr.next())
            A.copy(colT, sm[0:NCOL * SUPERS, 0:P]).then_inc(i_trc, 1)

            def project(parts):
                kin = D * len(parts)
                a.wait_ge(n_src, n_srcT.next())
                with loop(a, GROUPS, [(n_tp, 1)]) as g:
                    for q, part in enumerate(parts):
                        o = tmpP[:, 0:GB * kin].rearrange("p (b k) -> p b k", k=kin)[:, :, q * D:(q + 1) * D]
                        ins = A.copy(o, part[:, ds(g * (GB * D), GB * D)].rearrange("p (b k) -> p b k", k=D))
                    ins.then_inc(p_tmp, 1)
                    a.wait_ge(p_tp, n_tp.next())
                    A.copy(xT[0:kin, 0:4 * P], acc[0:kin, 0, :])
                    A.copy(xT[0:kin, 4 * P:GB * P], acc[0:kin, 1, 0:3 * P]).then_inc(p_xT, 1)

            def node_fn(fn, count=1):
                a.wait_ge(n_exp, t_n.next())
                fn().then_inc(n_expd, 1)

            t1 = big[:, 0:BLOCKS * D]
            sqrt = lambda: A.activation(nodev[:, 2, :], nodev[:, 1, :], ACT.Sqrt)

            for li, (kind, heads) in enumerate(PASSES):
                project([xN] if li in (0, 1, 3) else [hN])
                if heads:
                    pairs = -(-heads // 2)
                    nb = min(heads, 2)

                    def spread(k, j):
                        at = [0] + load_values(mybir.EngineType.Activation, k + 1, (CH - 1) * P, CH - 1)
                        a.wait_ge(l_ef[j % 2], efT[j % 2].next(16))
                        a.wait_ge(r_dve, t_rd.next())
                        hold(a)
                        for r in range(CH):
                            ins = A.copy(ef[:, j % 2, r, :], efRF[:, j % 2, ds(at[r], P)])
                        ins.then_inc(ef_rdy, 1)

                    def super_step(s, chunks):
                        if kind == "ef":
                            for j in range(chunks):
                                spread(s * SUPER + j * CH, j)
                        if kind == "dot":
                            a.wait_ge(acc_free, t_af.next())
                            hold(a)
                            for j in range(chunks):
                                a.wait_ge(g_row[j], rows[j].next(CH * 16))
                                A.copy(big[:, j * CH * D:(j + 1) * CH * D],
                                       slot(kind, j).rearrange("p s w -> p (s w)")).then_inc(r_act, 1)
                        for q in range(pairs):
                            a.wait_ge(tr_rdy, t_tr.next())
                            A.copy(R[:, q * 2:q * 2 + nb, :].rearrange("p h e -> p (h e)"),
                                   acc[:, q, 0:nb * P]).then_inc(tr_cp, 1)
                        a.wait_ge(f_arg, t_f.next())
                        A.activation(small4[0:heads, 1:2], small4[0:heads, 0:1], ACT.Exp).then_inc(f_exp, 1)
                        a.wait_ge(e_arg, t_e.next())
                        A.activation(R[:, 0:heads, :].rearrange("p h e -> p (h e)"),
                                     Mx[:, 0:heads, :].rearrange("p h e -> p (h e)"), ACT.Exp).then_inc(e_rdy, 1)
                        for q in range(pairs):
                            a.wait_ge(tr_rdy, t_tr.next())
                            A.copy(S[:, q * 2:q * 2 + nb, :].rearrange("p h e -> p (h e)"),
                                   acc[:, q, 0:nb * P]).then_inc(tr_cp, 1)

                    with loop(a, SUPERS - 1, [(t_tr, 2 * pairs), (t_e, 1), (t_f, 1)]
                              + ([(t_af, 1)] + [(t, CH * 16) for t in rows] if kind == "dot" else
                                 [(t, SCH // 2 * 16) for t in efT] + [(t_rd, SCH)])) as s:
                        super_step(s, SCH)
                    super_step(SUPERS - 1, LAST)
                if li == 0:
                    t_af.next(SUPERS)
                    for j in range(SLOTS):
                        rows[j].next((SUPERS - (j >= LAST)) * CH * 16)
                    project([xN, hN])
                    node_fn(sqrt)
                elif li == 1:
                    node_fn(lambda: A.activation(t1, t1, ACT.Exp))
                elif li in (2, 4):
                    node_fn(sqrt)
            project([xN])
            t_h = Tally(4 * CHUNKS)
            t_t = Tally(2)
            z = [Tally() for _ in range(2)]

            def keep_rows(j):
                a.wait_ge(d_rdy, t_h.next())
                A.copy(h_edge[:, j, :], acc[:, j, :]).then_inc(h_rdy, 1)

            def pair(first, last):
                for j in range(2):
                    if not (last and j):
                        keep_rows(1 - j)
                    a.wait_ge(t_rdy, t_t.next())
                    if not first:
                        a.wait_ge(w_tab[j], z[j].next(16 * CH))
                    A.copy(sums_out[:, j, :], acc[:, 2 + j, :]).then_inc(out_rdy, 1)

            keep_rows(0)
            pair(True, False)
            with loop(a, CHUNKS // 2 - 2, [(t_h, 2), (t_t, 2), (z[0], 16 * CH), (z[1], 16 * CH)]):
                pair(False, False)
            pair(False, True)
            node_fn(sqrt)

        @block.tensor
        def _(pe):
            t_hot, t_msg, t_df, t_s, t_tc, t_mr, t_ms, t_e, t_fr, t_acc = (Tally() for _ in range(10))
            n_tmp, n_xT, n_ev = Tally(), Tally(), Tally()
            rows = [Tally() for _ in range(SLOTS)]
            t_ef = Tally(2)

            pe.wait_ge(i_cntq, 1)
            T.matmul(sm[:, 0:2 * n48], ones, su[:, S_CF:S_CL + 1, :].rearrange("p a b -> p (a b)"),
                     start=True, stop=True).then_inc(i_cnt, 1)
            n = 0
            for src, ready in ((relF, (i_row, 2)), (valR, (i_row, 3)), (srcF, (i_row, 4)), (uR, (i_row, 5))):
                pe.wait_ge(*ready)
                for c in range(0, SUPERS, 4):
                    if n >= 4:
                        pe.wait_ge(i_trc, n - 3)
                    for q in range(min(4, SUPERS - c)):
                        ins = T.transpose(acc[:, n % 4, q * P:(q + 1) * P],
                                          src[:, (c + q) * P:(c + q + 1) * P], ident[:, :])
                    ins.then_inc(i_tr, 1)
                    n += 1
            T.transpose(sm[0:NCOL * SUPERS, 0:P], sk[:, K_COL:K_COL + NCOL, :].rearrange("p a b -> p (a b)"),
                        ident[:, :]).then_inc(i_tr, 1)

            pe.wait_ge(i_ready, 1)
            pe.wait_ge(i_w, 16 * W_LOADS)

            def project(kin, rhs, n_out, per_bank):
                with loop(pe, GROUPS, [(n_tmp, 1), (n_xT, 1), (n_ev, 1)]) as g:
                    pe.wait_ge(p_tmp, n_tmp.next())
                    hold(pe)
                    for j in range(GB):
                        ins = T.transpose(acc[0:kin, j // 4, (j % 4) * P:(j % 4 + 1) * P],
                                          tmpP[:, j * kin:(j + 1) * kin], ident[:, :])
                    ins.then_inc(p_tp, 1)
                    pe.wait_ge(p_xT, n_xT.next())
                    pe.wait_ge(p_ev, n_ev.next())
                    for j in range(GB):
                        o = (j % per_bank) * n_out
                        ins = T.matmul(acc[:, 2 + j // per_bank, o:o + n_out],
                                       xT[0:kin, j * P:(j + 1) * P], rhs, start=True, stop=True)
                    ins.then_inc(p_o, 1)

            def offsets(k):
                return load_values(mybir.EngineType.PE, k + STEPS, (GROUPS - 1) * BANK + (GB - 1) * AC)

            def open_acc():
                pe.wait_ge(acc_free, t_acc.next())
                pe.wait_ge(p_ev, n_ev.v + 1)
                for b in range(GROUPS):
                    T.matmul(acc[:, b, :], zeroW[:, :], zeroM[:, :], start=True, stop=False)

            def close_acc():
                for b in range(GROUPS):
                    ins = T.matmul(acc[:, b, :], zeroW[:, :], zeroM[:, :], start=False, stop=True)
                ins.then_inc(acc_rdy, 1)

            def add_chunk(k0, j, rhs, cols, needs_msg):
                at = offsets(k0)
                pe.wait_ge(hot_rdy, t_hot.next())
                if needs_msg:
                    pe.wait_ge(msg_rdy, t_msg.next())
                for r in range(CH):
                    ins = T.matmul(accF[:, ds(at[r], cols)], hot[:, j % 2, r * P:(r + 1) * P], rhs(r),
                                   start=False, stop=False)
                return ins

            for li, (kind, heads) in enumerate(PASSES):
                if kind == "ef":
                    project(D, rhs0[:, :], 66, GB)
                elif kind == "dot":
                    project(D, rhs1[:, li - 1, :], D, GB)
                else:
                    project(D, rhs2[:, li - 3, :], 3 * D, 2)
                if heads:
                    pairs = -(-heads // 2)
                    nb = min(heads, 2)
                    grp = 4 if kind == "ef" else 8
                    ng = CH // grp
                    cols = D + heads

                    def super_step(s, chunks):
                        lp = [(t_hot, 2), (t_df, 2 * ng)]
                        if kind == "ef":
                            lp += [(t_ef, 2)]
                        with loop(pe, chunks // 2, lp) as h:
                            for j in range(2):
                                at = offsets(s * SUPER + (h * 2 + j) * CH)
                                pe.wait_ge(hot_rdy, t_hot.next())
                                if kind == "ef":
                                    pe.wait_ge(ef_rdy, t_ef.next())
                                for g in range(ng):
                                    pe.wait_ge(d_free, t_df.next())
                                    for r in range(grp):
                                        st = g * grp + r
                                        o = at[st]
                                        if kind == "ef":
                                            d = acc[:, g, r * AC:(r + 1) * AC]
                                            T.matmul(d[:, 0:65], ef[:, j, st, :], rhsE[:, :], start=True, stop=True)
                                            ins = T.matmul(d[:, 65:68], hotB[:, j, st * P:(st + 1) * P],
                                                           dstB[:, ds(o * 2, 3)], start=True, stop=True)
                                        else:
                                            d = acc[:, j % 2, r * D:(r + 1) * D]
                                            ins = T.matmul(d, hot[:, j % 2, st * P:(st + 1) * P],
                                                           dstN[:, ds(o, D)], start=True, stop=True)
                                    ins.then_inc(d_rdy, 1)
                        pe.wait_ge(s_rdy, t_s.next())
                        for q in range(pairs):
                            for k in range(nb):
                                ins = T.transpose(acc[:, q, k * P:(k + 1) * P],
                                                  S[:, q * 2 + k, :], ident[:, :])
                            ins.then_inc(tr_rdy, 1)
                        pe.wait_ge(m_rows, t_mr.next())
                        hold(pe)
                        T.transpose(acc[0:heads, 2, 0:P], Mx[:, 0:heads, 0], ident[:, :])
                        T.transpose(acc[0:heads, 2, P:2 * P], Mx[:, 0:heads, P - 1],
                                    ident[:, :]).then_inc(m_rowsT, 1)
                        pe.wait_ge(m_seq, t_ms.next())
                        hold(pe)
                        sq = seqK[0:heads, 1, :].rearrange("h (r t) -> h r t", t=2)
                        T.transpose(acc[:, 3, 0:heads], sq[:, :, 0], ident[0:heads, 0:heads])
                        T.transpose(acc[:, 3, 4:4 + heads], sq[:, :, 1],
                                    ident[0:heads, 0:heads]).then_inc(m_seqT, 1)
                        pe.wait_ge(e_rdy, t_e.next())
                        for q in range(pairs):
                            for k in range(nb):
                                ins = T.transpose(acc[:, q, k * P:(k + 1) * P],
                                                  R[:, q * 2 + k, :], ident[:, :])
                            ins.then_inc(tr_rdy, 1)
                        pe.wait_ge(f_rhs, t_fr.next())
                        T.matmul(sm[:, 0:heads], hprev[0:heads, :], small4[0:heads, 4:4 + heads],
                                 start=True, stop=True).then_inc(f_all, 1)
                        pe.wait_ge(tr_cp, t_tc.next(2 * pairs))
                        open_acc()
                        with loop(pe, chunks // 2, [(t_hot, 2), (t_msg, 2)]) as h:
                            for j in range(2):
                                add_chunk(s * SUPER + (h * 2 + j) * CH, j,
                                          lambda r: msg[:, j, r, 0:cols], cols, True).then_inc(b_free, 1)
                        close_acc()

                    pers = [(t_hot, 2 * SCH), (t_msg, SCH), (t_df, ng * SCH), (t_s, 1), (t_mr, 1),
                            (t_ms, 1), (t_tc, 2 * pairs), (t_e, 1), (t_fr, 1), (t_acc, 1)]
                    if kind == "ef":
                        pers += [(t_ef, SCH)]
                    with loop(pe, SUPERS - 1, pers) as s:
                        super_step(s, SCH)
                    super_step(SUPERS - 1, LAST)
                else:
                    open_acc()
                    with loop(pe, CHUNKS // 2, [(t_hot, 2), (t_msg, 2)]) as i:
                        for j in range(2):
                            add_chunk((i * 2 + j) * CH, j, lambda r: msg[:, j, r, 0:65], 65,
                                      True).then_inc(b_free, 1)
                    close_acc()
                if kind == "ef":
                    project(2 * D, rhsO[:, :], D, GB)
            project(D, rhs3[:, :], D, GB)
            pe.wait_ge(p_ev, n_ev.v + 1)
            t_same, t_h, t_out = Tally(), Tally(), Tally()

            def edge_rows(k0, j):
                at = offsets(k0)
                pe.wait_ge(hot_rdy, t_hot.next())
                for r, o in enumerate(at):
                    ins = T.matmul(acc[:, j, r * D:(r + 1) * D], hot[:, j, r * P:(r + 1) * P],
                                   dstN[:, ds(o, D)], start=True, stop=True)
                ins.then_inc(d_rdy, 1)

            def pair(i, last):
                for j in range(2):
                    if not (last and j):
                        edge_rows(i * (2 * CH) + (j + 1) * CH, 1 - j)
                    pe.wait_ge(same_rdy, t_same.next())
                    pe.wait_ge(h_rdy, t_h.next())
                    for r in range(CH):
                        ins = T.matmul(acc[:, 2 + j, r * D:(r + 1) * D], same[:, j, r * P:(r + 1) * P],
                                       h_edge[:, j, r * D:(r + 1) * D], start=True, stop=True)
                    ins.then_inc(t_rdy, 1)

            edge_rows(0, 0)
            with loop(pe, CHUNKS // 2 - 1, [(t_hot, 2), (t_same, 2), (t_h, 2)]) as i:
                pair(i, False)
            pair(CHUNKS // 2 - 1, True)

        @block.vector
        def _(v):
            chain = Tally()

            def link(ins):
                ins.then_inc(dve, 1)
                v.wait_ge(dve, chain.next())

            t_b, t_d, t_tc, t_mT, t_sT, t_fe, t_fa, t_ar = (Tally() for _ in range(8))
            t_r = Tally(SLOTS)
            n_o, n_ex = Tally(), Tally()
            relT = [Tally() for _ in range(2)]
            rows = [Tally() for _ in range(SLOTS)]

            V.memset(xN[:, (BLOCKS - 1) * D:BLOCKS * D], 0.0)
            V.memset(nvS[:, BLOCKS - 1:BLOCKS], 0.0).then_inc(i_row, 1)
            V.memset(ones, 1.0)
            V.memset(zeroW[:, :], 0.0)
            V.memset(zeroM[:, :], 0.0)
            V.memset(prevrow[:, :, :], 0.0)
            link(V.memset(penF[:, :], -BIG))
            v.wait_ge(i_iota, 4)
            link(V.tensor_scalar(ident[:, :], iotaF[:, :], iotaP[:, 0:1], None, ALU.is_equal))
            v.wait_ge(i_dst, 16)
            dv = dstI.rearrange("p (c e) -> p c e", e=P)
            V.tensor_copy(firstlast[:, 0, :], dv[:, :, 0])
            link(V.tensor_copy(firstlast[:, 1, :], dv[:, :, P - 1]))
            cv = cmp.rearrange("p (b c) -> p b c", c=SUPERS)
            for q, to in ((0, S_CF), (1, S_CL)):
                link(V.tensor_tensor(cv, firstlast[:, q:q + 1, :].to_broadcast([P, n48, SUPERS]),
                                     su[:, S_B128, :].unsqueeze(2).to_broadcast([P, n48, SUPERS]), ALU.is_lt))
                link(V.tensor_reduce(su[:, to, :], cv, X, ALU.add))
            v.sem_inc(i_cntq, 1)
            v.wait_ge(i_cnt, 1)
            cf, cl = sm[:, 0:n48], sm[:, n48:2 * n48]
            link(V.tensor_copy(su[:, S_CL, :], cl))
            link(V.tensor_scalar(su[:, S_BM1, :], su[:, S_B128, :], 1.0 / P, -1.0, ALU.mult, ALU.add))
            link(V.tensor_tensor(su[:, S_RANK, :], cf, su[:, S_BM1, :], ALU.add))
            link(V.tensor_tensor(su[:, S_DEAD, :], cf, su[:, S_CL, :], ALU.is_equal))
            cv = cmp.rearrange("p (c b) -> p c b", b=n48)
            rank = su[:, S_RANK:S_RANK + 1, :].to_broadcast([P, SUPERS, n48])
            dead = su[:, S_DEAD:S_DEAD + 1, :].to_broadcast([P, SUPERS, n48])
            kk = sk[:, K_K, :].unsqueeze(2).to_broadcast([P, SUPERS, n48])
            link(V.tensor_tensor(cv, rank, kk, ALU.is_le))
            link(V.tensor_reduce(sk[:, K_B, :], cv, X, ALU.add))
            link(V.tensor_tensor(cv, rank, kk, ALU.is_equal))
            link(V.tensor_tensor(cv, cv, dead, ALU.mult))
            link(V.tensor_reduce(sk[:, K_DEAD, :], cv, X, ALU.add))
            tk = sk[:, K_COL + C_TILE, :]
            link(V.tensor_tensor(tk, sk[:, K_K, :], sk[:, K_B, :], ALU.subtract))
            link(V.tensor_scalar(tk, tk, 0.0, None, ALU.max))
            V.tensor_copy(tkI, tk).then_inc(i_tk, 1)
            base = sk[:, K_BASE, :]
            link(V.tensor_scalar(base, sk[:, K_DEAD, :], -float(1 << 16), None, ALU.mult))
            link(V.scalar_tensor_tensor(base, sk[:, K_B, :], float(P), base, ALU.mult, ALU.add))
            po = sk[:, K_COL + C_POFS, :]
            so = sk[:, K_COL + C_SOFS, :]
            link(V.tensor_scalar(po, sk[:, K_B, :], float(GB), None, ALU.is_ge))
            for m in range(2, GROUPS):
                link(V.scalar_tensor_tensor(po, sk[:, K_B, :], float(GB * m), po, ALU.is_ge, ALU.add))
            link(V.tensor_scalar(so, sk[:, K_B, :], float(AC), None, ALU.mult))
            link(V.scalar_tensor_tensor(po, po, float(BANK - GB * AC), so, ALU.mult, ALU.add))
            v.wait_ge(i_gd, 16 * SUPERS)
            link(V.tensor_copy(keyF, dstI))
            kv = keyF.rearrange("p (c e) -> p c e", e=P)
            rv = relF.rearrange("p (c e) -> p c e", e=P)
            vv = valR.rearrange("p (c e) -> p c e", e=P)
            link(V.tensor_tensor(rv, kv, base.unsqueeze(2).to_broadcast([P, SUPERS, P]), ALU.subtract))
            link(V.tensor_scalar(relF, relF, -1.0, float(P), ALU.max, ALU.min))
            V.tensor_copy(sk[:, K_COL + C_FIRST, :], kv[:, :, 0])
            V.tensor_copy(sk[:, K_COL + C_LAST, :], kv[:, :, P - 1])
            V.tensor_copy(sk[:, K_COL + C_RLAST, :], rv[:, :, P - 1])
            V.tensor_copy(relB, relF).then_inc(i_row, 1)
            link(V.tensor_scalar(valR, relF, 0.0, -1.0, ALU.is_ge, ALU.add))
            link(V.tensor_scalar(srcF, relF, float(P - 1), None, ALU.is_gt))
            link(V.tensor_tensor(valR, valR, srcF, ALU.subtract))
            V.tensor_scalar(valR, valR, BIG, None, ALU.mult).then_inc(i_row, 1)
            v.wait_ge(i_gs, 16 * SUPERS)
            V.tensor_copy(srcF, srcI).then_inc(i_row, 1)
            v.wait_ge(i_row, 4)

            def perm(to, node, high):
                link(V.tensor_scalar(to.bitcast(i32), node, P - 1, None, ALU.bitwise_and))
                link(V.tensor_scalar(high, node, P.bit_length() - 1, None, ALU.arith_shift_right))
                link(V.scalar_tensor_tensor(to, to.bitcast(i32), float(SB), high, ALU.mult, ALU.add))
                v.sem_inc(i_perm, 1)

            perm(permR, srcI, srcI)
            v.wait_ge(i_gu, 16 * SUPERS)
            V.tensor_scalar(uR, uR, 1.0, None, ALU.min).then_inc(i_row, 1)
            pv = penF[:, 0:STEPS].rearrange("p (c e) -> p c e", e=P)
            link(V.tensor_tensor(pv[:, :, 1:P], kv[:, :, 1:P], kv[:, :, 0:P - 1], ALU.not_equal))
            link(V.tensor_scalar(pv[:, :, 1:P], pv[:, :, 1:P], -BIG, None, ALU.mult))
            for pen, e in ((penA, 0), (penZ, P - 1)):
                q = pen[:, :].rearrange("p (c e) -> p c e", e=P)
                link(V.tensor_tensor(q, kv, kv[:, :, e:e + 1].to_broadcast([P, SUPERS, P]), ALU.not_equal))
                link(V.tensor_scalar(pen[:, :], pen[:, :], -BIG, None, ALU.mult))
            ngr = -(-SUPERS // 4)
            v.wait_ge(i_trc, 3 * ngr)
            V.tensor_copy(idxI, idxF).then_inc(i_idx, 1)
            v.wait_ge(i_idx, 1)
            perm(permC, idxI, idxF.bitcast(i32))
            v.wait_ge(i_ld, 16 * 6)
            first, last = firstR, lastR
            pr = penR[:, 0:2 * STEPS].rearrange("h (k t) -> h k t", t=2)
            V.memset(penR[:, 2 * STEPS:2 * STEPS + 1], -BIG)
            V.memset(pr[:, 0:1, 0], -BIG)
            link(V.tensor_tensor(pr[:, 1:STEPS, 0], first[:, 1:STEPS], last[:, 0:STEPS - 1], ALU.not_equal))
            link(V.tensor_tensor(pr[:, :, 1], first, last, ALU.not_equal))
            link(V.tensor_scalar(pr[:, 1:STEPS, 0], pr[:, 1:STEPS, 0], -BIG, None, ALU.mult))
            link(V.tensor_scalar(pr[:, :, 1], pr[:, :, 1], -BIG, None, ALU.mult))
            link(V.tensor_copy(prevofs[:, :], prevrow[0:1, 1, :]))
            v.wait_ge(i_sc, 80)
            V.memset(linN[:, :], 0.0)
            link(V.memset(dstN[:, :], 0.0))
            tile = rows33[32:33, 0:STEPS].rearrange("o (c r) -> o c r", r=CH)
            link(V.tensor_tensor(tile[:, :, 1:CH], tile[:, :, 1:CH],
                                 tile[:, :, 0:1].to_broadcast([1, STEPS // CH, CH - 1]), ALU.subtract))
            link(V.tensor_scalar(tile[:, :, 1:CH], tile[:, :, 1:CH], float(P), None, ALU.mult))
            V.tensor_copy(offs, rows33[32:33, 0:2 * STEPS]).then_inc(i_ready, 1)
            for s, k in ((d_free, 2), (b_free, 2), (ef_rdy, 2), (acc_free, 1), (p_ev, 1),
                         (r_dve, SLOTS), (r_act, SLOTS)):
                v.sem_inc(s, k)
            v.wait_ge(i_w, 16 * W_LOADS)

            big3 = big[:, 0:BLOCKS * D].rearrange("p (b d) -> p b d", d=D)
            t1 = big[:, 0:BLOCKS * D]
            t2 = big[:, BLOCKS * D:2 * BLOCKS * D]
            x3 = xN[:, :].rearrange("p (b d) -> p b d", d=D)
            acc3 = accS[:, :].rearrange("p (b c) -> p b c", c=AC)
            accP = acc[:, :, 0:GB * AC]
            accS4 = accS[:, :].rearrange("p (g c) -> p g c", g=GROUPS)
            h3 = hN[:, :].rearrange("p (b d) -> p b d", d=D)
            l3 = linN[:, :].rearrange("p (b d) -> p b d", d=D)

            def layer_norm(resid):
                m, var, sd = nodev[:, 0, :], nodev[:, 1, :], nodev[:, 2, :]
                bc = lambda a: a.unsqueeze(2).to_broadcast([P, BLOCKS, D])
                t2v = t2.rearrange("p (b d) -> p b d", d=D)
                link(V.tensor_tensor(xN[:, :], xN[:, :], resid, ALU.add))
                link(V.tensor_reduce(m, x3, X, ALU.add))
                link(V.tensor_scalar(m, m, 1.0 / D, None, ALU.mult))
                link(V.tensor_tensor(x3, x3, bc(m), ALU.subtract))
                link(V.tensor_tensor(t2, xN[:, :], xN[:, :], ALU.mult))
                link(V.tensor_reduce(var, t2v, X, ALU.add))
                V.tensor_scalar(var, var, 1.0 / D, LN_EPS, ALU.mult, ALU.add).then_inc(n_exp, 1)
                v.wait_ge(n_expd, n_ex.next())
                link(V.reciprocal(m, sd))
                link(V.tensor_tensor(x3, x3, bc(m), ALU.mult))

            def divide(heads):
                d = den4[:, :, 0:heads]
                link(V.tensor_scalar(d, acc3[:, :, D:D + heads], 1e-30, None, ALU.max))
                link(V.reciprocal(d, d))
                if heads == 1:
                    link(V.tensor_tensor(h3, acc3[:, :, 0:D], d.to_broadcast([P, BLOCKS, D]), ALU.mult))
                else:
                    for q in range(heads):
                        w = D // heads
                        ins = V.tensor_tensor(h3[:, :, q * w:(q + 1) * w], acc3[:, :, q * w:(q + 1) * w],
                                              d[:, :, q:q + 1].to_broadcast([P, BLOCKS, w]), ALU.mult)
                    link(ins)

            def start_projection():
                v.sem_inc(n_src, 1)

            def project(evacuate):
                with loop(v, GROUPS, [(n_o, 1)]) as g:
                    v.wait_ge(p_o, n_o.next())
                    evacuate(g).then_inc(p_ev, 1)

            def evac_ef(g):
                o = acc[:, 2, 0:GB * 66].rearrange("p (b w) -> p b w", w=66)
                V.tensor_copy(nodev[:, 3, ds(g * GB, GB)], o[:, :, 65])
                return V.tensor_copy(big[:, ds(g * (GB * 65), GB * 65)].rearrange("p (b w) -> p b w", w=65),
                                     o[:, :, 0:65])

            def evac_dot(g):
                o = acc[:, 2, 0:GB * D].rearrange("p (b w) -> p b w", w=D)
                V.tensor_copy(dstN[:, ds(g * BANK, GB * AC)].rearrange("p (b c) -> p b c", c=AC)[:, :, 0:D], o)
                return V.tensor_copy(big[:, ds(g * (GB * D), GB * D)].rearrange("p (b w) -> p b w", w=D), o)

            def evac_spline(g):
                for lo, n, o in ((0, 6, acc[:, 2:5, 0:6 * D]), (6, 1, acc[:, 5:6, 0:3 * D])):
                    lin = linN[:, ds(g * (GB * D) + lo * D, n * D)]
                    st = big[:, ds(g * (GB * 2 * D) + lo * 2 * D, n * 2 * D)]
                    if n == 6:
                        o4 = o.rearrange("p a (b w) -> p a b w", w=3 * D)
                        V.tensor_copy(lin.rearrange("p (a b w) -> p a b w", b=2, w=D), o4[:, :, :, 2 * D:])
                        V.tensor_copy(st.rearrange("p (a b w) -> p a b w", b=2, w=2 * D), o4[:, :, :, 0:2 * D])
                    else:
                        V.tensor_copy(lin, o[:, 0, 2 * D:])
                        ins = V.tensor_copy(st, o[:, 0, 0:2 * D])
                return ins

            def evac_sum(g):
                o = acc[:, 2, 0:GB * D].rearrange("p (b w) -> p b w", w=D)
                return V.tensor_tensor(dstN[:, ds(g * BANK, GB * AC)].rearrange("p (b c) -> p b c", c=AC)[:, :, 0:D], o,
                                       nvS[:, ds(g * GB, GB)].unsqueeze(2).to_broadcast([P, GB, D]), ALU.mult)

            def evac_out(g):
                return V.tensor_scalar(t1[:, ds(g * (GB * D), GB * D)], acc[:, 2, 0:GB * D], 0.0, None, ALU.max)

            def one_hot_nodes(j, to):
                v.wait_ge(l_rel[j % 2], relT[j % 2].next(16))
                V.tensor_scalar(to[:, j % 2, :], relrow[:, j % 2, :], iotaP[:, 0:1], None,
                                ALU.is_equal).then_inc(hot_rdy, 1)

            def one_hot_edges(k0, j):
                v.wait_ge(b_free, t_b.next())
                V.tensor_tensor(hot[:, j % 2, :].rearrange("p (s n) -> p s n", n=P),
                                iotaF[:, :].unsqueeze(1).to_broadcast([P, CH, P]),
                                relC[:, ds(k0, CH)].unsqueeze(2).to_broadcast([P, CH, P]),
                                ALU.is_equal).then_inc(hot_rdy, 1)

            def scores(kind, j):
                v.wait_ge(g_row[j], rows[j].next(CH * 16))
                if kind == "ef":
                    for g in range(2):
                        v.wait_ge(d_rdy, t_d.next())
                        k = j * CH + 4 * g
                        d = acc[:, g, 0:4 * AC].rearrange("p (s c) -> p s c", c=AC)
                        V.tensor_tensor(big[:, k * 65:(k + 4) * 65].rearrange("p (s w) -> p s w", w=65),
                                        d[:, :, 0:65], slot(kind, j)[:, 4 * g:4 * g + 4, :], ALU.add)
                        V.tensor_reduce(S[:, 1, k:k + 4], d[:, :, 65:68], X, ALU.add).then_inc(d_free, 1)
                    v.wait_ge(d_free, t_d.v + 2)
                    v.sem_inc(r_dve, 1)
                    t_r.next()
                else:
                    v.wait_ge(r_dve, t_r.v)
                    v.wait_ge(d_rdy, t_d.next())
                    V.scalar_tensor_tensor(prod, acc[:, j % 2, :], 0.25,
                                           slot(kind, j).rearrange("p s w -> p (s w)"),
                                           ALU.mult, ALU.mult).then_inc(d_free, 1)
                    v.wait_ge(d_free, t_d.v + 2)
                    so = S[:, :, j * CH:(j + 1) * CH].rearrange("p h s -> p s h")
                    V.tensor_reduce(so, prod.rearrange("p (s h w) -> p s h w", h=4, w=16), X,
                                    ALU.add).then_inc(r_dve, 1)
                    t_r.next()

            def attention(kind, heads, n_links):
                bw = ROWS if kind == "ef" else D
                ng = 2 if kind == "ef" else 1
                if kind == "ef":
                    node, part = nodev[:, 3, :], nodev[:, 0, :]
                    b4 = dstB.rearrange("p (g w) -> p g w", w=2 * BANK)[:, :, 0:2 * GB * AC].rearrange(
                        "p g (b c) -> p g b c", c=2 * AC)
                    nv4 = node.rearrange("p (g b) -> p g b", b=GB)
                    pt4 = part.rearrange("p (g b) -> p g b", b=GB)
                    v.wait_ge(p_ev, n_o.v + 1)
                    for q in range(3):
                        link(V.tensor_copy(b4[:, :, :, q], nv4))
                        if q < 2:
                            link(V.tensor_copy(pt4, b4[:, :, :, q]))
                            link(V.tensor_tensor(node, node, part, ALU.subtract))
                link(V.memset(accS[:, :], 0.0))
                link(V.memset(carry[:, :], -BIG))
                pairs, w = -(-heads // 2), D // heads

                def super_step(s, chunks):
                    to = hotB if kind == "ef" else hot
                    one_hot_nodes(0, to)
                    for j in range(chunks):
                        if j + 1 < chunks:
                            one_hot_nodes(j + 1, to)
                        scores(kind, j)
                    hd = range(heads)
                    inv = invC[:, ds(s * SUPER, SUPER)]
                    if kind == "ef":
                        sc = big[:, :].rearrange("p (s w) -> p s w", w=ROWS)[:, :, D]
                        link(V.scalar_tensor_tensor(S[:, 2, :], sc, battn[:, 0:1], S[:, 1, :], ALU.add, ALU.add))
                        link(V.scalar_tensor_tensor(S[:, 0, :], S[:, 2, :], 0.01, S[:, 2, :], ALU.mult, ALU.max))
                    else:
                        v.wait_ge(r_dve, t_r.v)
                    V.tensor_tensor(S[:, 0:heads, :], S[:, 0:heads, :],
                                    inv.unsqueeze(1).to_broadcast([P, heads, P]), ALU.add).then_inc(s_rdy, 1)
                    v.wait_ge(tr_cp, t_tc.next(pairs))
                    pf, pq = penS, penRS[0:heads, :]
                    V.tensor_copy(pf, penF[:, ds(s * P, P + 1)])
                    link(V.tensor_copy(pq, penR[0:heads, ds(s * (2 * P), 2 * P + 1)]))
                    for q in hd:
                        link(V.tensor_tensor_scan(Fm[:, q, :], pf[:, 0:P], R[:, q, :], -BIG, op0=ALU.add, op1=ALU.max))
                    for q in hd:
                        ins = V.tensor_tensor_scan(Mx[:, q, ::-1], pf[:, P:0:-1], Fm[:, q, ::-1], -BIG,
                                                   op0=ALU.add, op1=ALU.max)
                    ins.then_inc(m_rows, 1)
                    v.wait_ge(m_rowsT, t_mT.next())
                    q0 = seqK[0:heads, 0, :].rearrange("h (r t) -> h r t", t=2)
                    V.tensor_copy(q0[:, :, 0], acc[0:heads, 2, 0:P])
                    link(V.tensor_copy(q0[:, :, 1], acc[0:heads, 2, P:2 * P]))
                    link(V.tensor_tensor_scan(seqK[0:heads, 0, :], pq[:, 0:2 * P], seqK[0:heads, 0, :],
                                              carry[0:heads, :], op0=ALU.add, op1=ALU.max))
                    V.tensor_tensor_scan(seqK[0:heads, 1, ::-1], pq[:, 2 * P:0:-1], seqK[0:heads, 0, ::-1],
                                         -BIG, op0=ALU.add, op1=ALU.max).then_inc(m_seq, 1)
                    v.wait_ge(m_seqT, t_sT.next())
                    link(V.tensor_copy(AZ[:, :, 0:heads],
                                       acc[:, 3, 0:8].rearrange("p (t h) -> p t h", h=4)[:, :, 0:heads]))
                    for t, pen in ((0, penA), (1, penZ)):
                        for q in hd:
                            link(V.scalar_tensor_tensor(Mx[:, q, :], pen[:, ds(s * P, P)], AZ[:, t, q:q + 1],
                                                        Mx[:, q, :], ALU.add, ALU.max))
                    V.tensor_tensor(Mx[:, 0:heads, :], R[:, 0:heads, :], Mx[:, 0:heads, :],
                                    ALU.subtract).then_inc(e_arg, 1)
                    link(V.tensor_tensor(small4[0:heads, 2:3], carry[0:heads, :], seqK[0:heads, 1, 0:1], ALU.subtract))
                    V.tensor_scalar(small4[0:heads, 0:1], small4[0:heads, 2:3], 0.0, None,
                                    ALU.min).then_inc(f_arg, 1)
                    link(V.tensor_copy(carry[0:heads, :], seqK[0:heads, 1, 2 * P - 1:2 * P]))
                    link(V.tensor_scalar(small4[0:heads, 3:4], pq[:, 0:1], 0.0, None, ALU.is_equal))
                    link(V.tensor_copy(small4[0:heads, 8:9], prevrow[0:heads, 0, ds(s, 1)]))
                    link(V.tensor_scalar(hprev[0:heads, :], iotaF[0:heads, :], small4[0:heads, 8:9], None,
                                         ALU.is_equal))
                    v.wait_ge(f_exp, t_fe.next())
                    link(V.tensor_scalar(small4[0:heads, 2:3], small4[0:heads, 1:2], -1.0, None, ALU.add))
                    link(V.tensor_tensor(small4[0:heads, 2:3], small4[0:heads, 2:3], small4[0:heads, 3:4], ALU.mult))
                    V.tensor_scalar(small4[0:heads, 4:4 + heads], ident[0:heads, 0:heads],
                                    small4[0:heads, 2:3], None, ALU.mult).then_inc(f_rhs, 1)
                    v.wait_ge(tr_cp, t_tc.next(pairs))
                    v.wait_ge(f_all, t_fa.next())
                    link(V.tensor_scalar(fac[:, 0:heads], sm[:, 0:heads], 1.0, None, ALU.add))
                    hold(v)
                    with loop(v, chunks // 2, [(t_b, 2)]) as h:
                        for j in range(2):
                            k = (h * 2 + j) * CH
                            one_hot_edges(s * SUPER + k, j)
                            b = big[:, ds(k * bw, CH * bw)].rearrange("p (s w) -> p s w", w=bw)
                            ex = S[:, 0:heads, ds(k, CH)].rearrange("p h s -> p s h")
                            V.tensor_copy(msg[:, j, :, D:D + heads], ex)
                            for q in hd:
                                ins = V.tensor_tensor(msg[:, j, :, q * w:(q + 1) * w], b[:, :, q * w:(q + 1) * w],
                                                      ex[:, :, q:q + 1].to_broadcast([P, CH, w]), ALU.mult)
                            ins.then_inc(msg_rdy, 1)
                    hold(v)
                    o = v.value_load(prevofs[0:1, ds(s, 1)], min_val=0, max_val=(BLOCKS - 1) * AC)
                    for q in hd:
                        part = accS[:, ds(o + q * w, w)]
                        V.tensor_scalar(part, part, fac[:, q:q + 1], None, ALU.mult)
                    part = accS[:, ds(o + D, heads)]
                    link(V.tensor_tensor(part, part, fac[:, 0:heads], ALU.mult))
                    v.wait_ge(acc_rdy, t_ar.next())
                    link(V.tensor_tensor(accS4, accS4, accP, ALU.add))
                    v.sem_inc(acc_free, 1)

                pers = [(chain, n_links), (t_b, SCH), (t_d, ng * SCH), (t_tc, 2 * pairs), (t_mT, 1), (t_sT, 1),
                        (t_fe, 1), (t_fa, 1), (t_r, SCH), (t_ar, 1), (relT[0], SCH * 8), (relT[1], SCH * 8)]
                with loop(v, SUPERS - 1, pers + [(t, CH * 16) for t in rows]) as s:
                    super_step(s, SCH)
                super_step(SUPERS - 1, LAST)

            def linear(kind, li):
                use = USE[kind]

                def chunk(k, j):
                    one_hot_edges(k, j)
                    v.wait_ge(g_row[j], rows[j].next(CH * 16))
                    z = slot(kind, j)
                    m = msg[:, j % 2, :, 0:D]
                    V.tensor_tensor(m, z[:, :, 0:D], invC[:, ds(k, CH)].unsqueeze(2).to_broadcast([P, CH, D]),
                                    ALU.mult)
                    pv = (prod, prod2)[j % 2].rearrange("p (s w) -> p s w", w=D)
                    V.tensor_tensor(pv, z[:, :, D:2 * D],
                                    uC[:, ds(k, CH)].unsqueeze(2).to_broadcast([P, CH, D]),
                                    ALU.mult).then_inc(r_dve, 1)
                    v.wait_ge(r_dve, t_r.next())
                    V.tensor_tensor(m, m, pv, ALU.add).then_inc(msg_rdy, 1)

                with loop(v, CHUNKS // use, [(t_b, use), (t_r, use)] +
                          [(rows[j], CH * 16) for j in range(use)]) as i:
                    for j in range(use):
                        chunk(i * (use * CH) + j * CH, j)
                for j in range(CHUNKS % use):
                    chunk((CHUNKS // use * use + j) * CH, j)
                v.wait_ge(acc_rdy, t_ar.next())
                link(V.tensor_copy(accS4, accP))
                v.sem_inc(acc_free, 1)

            start_projection()
            project(evac_ef)
            attention("ef", 1, LINKS[1])
            divide(1)
            start_projection()
            project(evac_out)
            v.wait_ge(p_ev, n_o.v + 1)
            layer_norm(t1)
            start_projection()
            project(evac_dot)
            attention("dot", 4, LINKS[4])
            divide(4)
            V.tensor_scalar(t1, hN[:, :], 0.0, None, ALU.min).then_inc(n_exp, 1)
            link(V.tensor_scalar(hN[:, :], hN[:, :], 0.0, -1.0, ALU.max, ALU.add))
            v.wait_ge(n_expd, n_ex.next())
            link(V.tensor_tensor(hN[:, :], hN[:, :], t1, ALU.add))
            start_projection()
            project(evac_dot)
            attention("dot", 4, LINKS[4])
            divide(4)
            layer_norm(hN[:, :])
            link(V.tensor_scalar(invC[:, :], uC[:, :], -1.0, 1.0, ALU.mult, ALU.add))
            link(V.memset(msg[:, :, :, D:D + 1], 1.0))
            v.wait_ge(z_tab, 16 * 2 * TABLES)
            for li in (3, 4):
                start_projection()
                project(evac_spline)
                v.wait_ge(p_ev, n_o.v + 1)
                link(V.tensor_tensor(l3, l3, biasS[:, li - 3:li - 2, :].to_broadcast([P, BLOCKS, D]), ALU.add))
                linear("spline", li)
                if li == 3:
                    link(V.tensor_scalar(rcnt[:, :], acc3[:, :, D], 1.0, None, ALU.max))
                    link(V.reciprocal(rcnt[:, :], rcnt[:, :]))
                link(V.tensor_tensor(h3, acc3[:, :, 0:D], rcnt[:, :].unsqueeze(2).to_broadcast([P, BLOCKS, D]),
                                     ALU.mult))
                link(V.tensor_tensor(hN[:, :], hN[:, :], linN[:, :], ALU.add))
                link(V.tensor_scalar(hN[:, :], hN[:, :], 0.0, None, ALU.max))
            layer_norm(hN[:, :])
            v.sem_inc(k_room, 1)
            start_projection()
            project(evac_sum)
            v.wait_ge(p_ev, n_o.v + 1)
            v.sem_inc(k_free, 2)
            v.sem_inc(t_rdy, 2)
            V.tensor_scalar(tri, iotaF[:, :], iotaP[:, 0:1], None, ALU.is_lt)
            link(V.tensor_scalar(spare, iotaP[:, 0:1], float(SB), float(BLOCKS), ALU.mult, ALU.add))
            v.wait_ge(k_col, 16)
            t_h, t_t, t_same = Tally(4 * CHUNKS - 2), Tally(), Tally()
            keyT = [Tally() for _ in range(2)]
            z = [Tally() for _ in range(2)]
            def keys(i, first):
                for j in range(2):
                    key = keyC[:, ds(i * (2 * CH) + j * CH, CH)]
                    v.wait_ge(d_rdy, t_h.next())
                    one_hot_nodes(j, hot)
                    v.wait_ge(l_key[j], keyT[j].next(16))
                    v.wait_ge(t_rdy, t_t.next())
                    V.tensor_tensor(same[:, j, :].rearrange("p (s e) -> p s e", e=P),
                                    keyrow[:, j, :].rearrange("p (s e) -> p s e", e=P),
                                    key.unsqueeze(2).to_broadcast([P, CH, P]), ALU.is_equal).then_inc(same_rdy, 1)
                    v.wait_ge(same_rdy, t_same.next())
                    v.sem_inc(k_free, 1)
                    link(V.tensor_tensor(waste.rearrange("p (s e) -> p s e", e=P),
                                         same[:, j, :].rearrange("p (s e) -> p s e", e=P),
                                         tri.unsqueeze(1).to_broadcast([P, CH, P]), ALU.mult))
                    link(V.tensor_reduce(seen, waste.rearrange("p (s e) -> p s e", e=P), X, ALU.max))
                    link(V.tensor_scalar(keep, key, -1.0, spare, ALU.mult, ALU.add))
                    link(V.tensor_tensor(keep, keep, seen, ALU.mult))
                    link(V.tensor_tensor(keep, keep, key, ALU.add))
                    if not first:
                        v.wait_ge(w_tab[j], z[j].next(16 * CH))
                    V.tensor_copy(idxb[:, j, :], keep).then_inc(idx_rdy, 1)

            keys(0, True)
            with loop(v, CHUNKS // 2 - 1, [(t_h, 2), (t_t, 2), (t_same, 2), (chain, 2 * 5)]
                      + [(t, 16 * CH) for t in z] + [(t, 16) for t in relT + keyT]) as i:
                keys(i + 1, False)
            v.wait_ge(idx_rdy, CHUNKS)
            v.sem_inc(t_use, 2)
            for t in range(TABLES):
                v.wait_ge(t_ld[t % 2], 16 * (t // 2 + 1))
                if t:
                    link(V.tensor_tensor(hN[:, :], hN[:, :], sumsT[:, t % 2, :], ALU.add))
                else:
                    link(V.tensor_copy(hN[:, :], sumsT[:, 0, :]))
                v.sem_inc(t_use, 1)
            h4 = hN[:, :].rearrange("p (g b d) -> p g b d", b=GB, d=D)
            own = dstN[:, :].rearrange("p (g w) -> p g w", w=BANK)[:, :, 0:GB * AC].rearrange(
                "p g (b c) -> p g b c", c=AC)[:, :, :, 0:D]
            link(V.tensor_tensor(h4, h4, own, ALU.add))
            layer_norm(hN[:, :])
            v.sem_inc(o_rdy, 1)


def kernel(x, src, dst, edge_attr_64, edge_weight1, node_vec, L0_gnn_W_ne, L0_gnn_W_attn, L0_gnn_b_attn,
           L0_gnn_W_out, L1_gnn_W1, L1_gnn_W2, L2_gnn_W1, L2_gnn_lw1, L2_gnn_b1, L2_gnn_W2, L2_gnn_lw2,
           L2_gnn_b2, L3_gnn_W):
    import numpy as np
    import concourse.bacc as bacc
    from concourse.bass_utils import run_bass_kernel_spmd

    def tiles(a, fill, count):
        a = np.asarray(a)
        o = np.full((count * P,) + a.shape[1:], fill, a.dtype)
        o[:N_EDGES] = a
        return o.reshape((count, P) + a.shape[1:])

    arrays = [
        ("x", np.asarray(x)),
        ("src", tiles(src, 0, TILES_PAD)),
        ("dst", tiles(dst, PAD_NODE, TILES_PAD)),
        ("u", tiles(edge_weight1, 0, TILES_PAD)[:, :, 0]),
        ("eft", tiles(edge_attr_64, 0, EF_TILES).transpose(0, 2, 1)),
        ("nv", np.asarray(node_vec)),
        ("w_ne", np.asarray(L0_gnn_W_ne)), ("w_attn", np.asarray(L0_gnn_W_attn)),
        ("b_attn", np.asarray(L0_gnn_b_attn)), ("w_out", np.asarray(L0_gnn_W_out)),
        ("w1t", np.asarray(L1_gnn_W1).T), ("w2t", np.asarray(L1_gnn_W2).T),
        ("s_w1", np.asarray(L2_gnn_W1)), ("s_lw1", np.asarray(L2_gnn_lw1)), ("s_b1", np.asarray(L2_gnn_b1)),
        ("s_w2", np.asarray(L2_gnn_W2)), ("s_lw2", np.asarray(L2_gnn_lw2)), ("s_b2", np.asarray(L2_gnn_b2)),
        ("w3t", np.asarray(L3_gnn_W).T),
    ]
    nc = bacc.Bacc("TRN2", target_bir_lowering=False, num_devices=1)
    feed, args = {}, []
    for name, a in arrays:
        a = np.ascontiguousarray(a)
        feed[f"{name}_dram"] = a
        args.append(nc.dram_tensor(f"{name}_dram", a.shape, mybir.dt.from_np(a.dtype), kind="ExternalInput").ap())
    args.append(nc.dram_tensor("out_dram", (N_NODES, D), mybir.dt.float32, kind="ExternalOutput").ap())
    gnn(nc, *args)
    r = run_bass_kernel_spmd(nc, [feed], core_ids=[0])
    return r.results[0]["out_dram"]
```
